# Optimizing a Trainium2 kernel written in Bass

```python
import numpy as np
import jax
import jax.numpy as jnp

def _softmax(x, axis=-1):
    return jax.nn.softmax(x, axis=axis)

def _gelu(x):
    return jax.nn.gelu(x, approximate=True)

def _silu(x):
    return jax.nn.silu(x)

def _sigmoid(x):
    return jax.nn.sigmoid(x)

def _layernorm(x, axis=-1, eps=1e-05):
    m = jnp.mean(x, axis=axis, keepdims=True)
    v = jnp.var(x, axis=axis, keepdims=True)
    return (x - m) / jnp.sqrt(v + eps)

def _scatter_add(tgt, idx, src, axis=0):
    return tgt.at[idx].add(src)

def _segment_sum(src, seg, n):
    return jax.ops.segment_sum(src, seg, n)
kernel_name = 'mk_cond_resid_d2_seqx_r2_6880ef'

def setup_inputs(seed: int=0):
    np.random.seed(seed)
    _w = jnp.asarray

    def _rec_inputs():
        import jax
        import jax.numpy as jnp
        _rk = jax.random.key(seed)
        x = -0.000125 + 0.9999 * jax.random.normal(jax.random.fold_in(_rk, 1), (2, 2048, 512), jnp.float32)
        _lenS = 2048 - jax.random.randint(jax.random.fold_in(_rk, 7), (2,), 0, max(1, 2048 // 4) + 1, jnp.int32)
        _lenS2 = 2048 - jax.random.randint(jax.random.fold_in(_rk, 8), (2,), 0, max(1, 2048 // 4) + 1, jnp.int32)
        cond_1024 = 0.00782532 + 1.00527 * jax.random.normal(jax.random.fold_in(_rk, 11), (2, 512), jnp.float32)
        return (x, cond_1024)
    x, cond_1024 = _rec_inputs()

    def _L0_cond_setup():
        import jax, jax.numpy as jnp
        import numpy as np
        INV_SQRT2 = 0.7071067811865476
        key = jax.random.key(seed)
        k1, k2, k3, k4 = jax.random.split(key, 4)
        B, N, d = (8, 2048, 512)
        scale = 1.0 / np.sqrt(d)
        return {'v': jax.random.normal(k1, (B, N, d), dtype=jnp.float32), 'q_pool': jax.random.normal(k2, (B, d), dtype=jnp.float32), 'W1': jax.random.normal(k3, (d, d), dtype=jnp.float32) * scale, 'b1': jnp.zeros((d,), dtype=jnp.float32), 'W2': jax.random.normal(k4, (d, d), dtype=jnp.float32) * scale, 'b2': jnp.zeros((d,), dtype=jnp.float32)}
    _L0_cond_all = _L0_cond_setup()
    _L0_cond_in = {k: v for k, v in _L0_cond_all.items() if k in ('W1', 'b1', 'W2', 'b2')}
    del _L0_cond_all

    def _L1_cond_setup():
        import jax, jax.numpy as jnp
        import numpy as np
        B, T, D_IN, V_IN, E = (64, 128, 512, 512, 512)
        key = jax.random.key(seed)
        ks = jax.random.split(key, 16)
        s = 0.01
        return {'video': jax.random.normal(ks[0], (B, V_IN), jnp.float32), 'seq': jax.random.normal(ks[1], (B, T, D_IN), jnp.float32), 'W_z': jax.random.normal(ks[2], (D_IN, E), jnp.float32) * s, 'U_z': jax.random.normal(ks[3], (E, E), jnp.float32) * s, 'C_z': jax.random.normal(ks[4], (V_IN, E), jnp.float32) * s, 'b_z': jnp.zeros((E,), jnp.float32), 'W_r': jax.random.normal(ks[5], (D_IN, E), jnp.float32) * s, 'U_r': jax.random.normal(ks[6], (E, E), jnp.float32) * s, 'C_r': jax.random.normal(ks[7], (V_IN, E), jnp.float32) * s, 'b_r': jnp.zeros((E,), jnp.float32), 'W': jax.random.normal(ks[8], (D_IN, E), jnp.float32) * s, 'U': jax.random.normal(ks[9], (E, E), jnp.float32) * s, 'C': jax.random.normal(ks[10], (V_IN, E), jnp.float32) * s, 'b': jnp.zeros((E,), jnp.float32)}
    _L1_cond_all = _L1_cond_setup()
    _L1_cond_in = {k: v for k, v in _L1_cond_all.items() if k in ('W_z', 'U_z', 'C_z', 'b_z', 'W_r', 'U_r', 'C_r', 'b_r', 'W', 'U', 'C', 'b')}
    del _L1_cond_all
    return {'x': x, 'cond_1024': cond_1024, 'L0_cond_W1': _L0_cond_in['W1'], 'L0_cond_b1': _L0_cond_in['b1'], 'L0_cond_W2': _L0_cond_in['W2'], 'L0_cond_b2': _L0_cond_in['b2'], 'L1_cond_W_z': _L1_cond_in['W_z'], 'L1_cond_U_z': _L1_cond_in['U_z'], 'L1_cond_C_z': _L1_cond_in['C_z'], 'L1_cond_b_z': _L1_cond_in['b_z'], 'L1_cond_W_r': _L1_cond_in['W_r'], 'L1_cond_U_r': _L1_cond_in['U_r'], 'L1_cond_C_r': _L1_cond_in['C_r'], 'L1_cond_b_r': _L1_cond_in['b_r'], 'L1_cond_W': _L1_cond_in['W'], 'L1_cond_U': _L1_cond_in['U'], 'L1_cond_C': _L1_cond_in['C'], 'L1_cond_b': _L1_cond_in['b']}

def reference(x, cond_1024, L0_cond_W1, L0_cond_b1, L0_cond_W2, L0_cond_b2, L1_cond_W_z, L1_cond_U_z, L1_cond_C_z, L1_cond_b_z, L1_cond_W_r, L1_cond_U_r, L1_cond_C_r, L1_cond_b_r, L1_cond_W, L1_cond_U, L1_cond_C, L1_cond_b):
    import jax
    import jax.numpy as jnp

    def _L0_cond_ref(v, q_pool, W1, b1, W2, b2):
        import jax, jax.numpy as jnp
        import numpy as np
        INV_SQRT2 = 0.7071067811865476
        B, N, d = v.shape
        h = jax.nn.silu(q_pool @ W1.T + b1)
        gate = jax.nn.sigmoid(h @ W2.T + b2)[:, None, :]
        levels = int(np.log2(N))
        a = v
        details = []
        for _ in range(levels):
            e, o = (a[:, 0::2], a[:, 1::2])
            details.append((e - o) * INV_SQRT2)
            a = (e + o) * INV_SQRT2
        a = a * gate
        for dc in reversed(details):
            dc = dc * gate
            e = (a + dc) * INV_SQRT2
            o = (a - dc) * INV_SQRT2
            n = e.shape[1]
            a = jnp.stack([e, o], axis=2).reshape(B, 2 * n, d)
        return v + a

    def _L1_cond_ref(video, seq, W_z, U_z, C_z, b_z, W_r, U_r, C_r, b_r, W, U, C, b):
        import jax, jax.numpy as jnp
        import numpy as np
        B, T, D_IN, V_IN, E = (64, 128, 512, 512, 512)
        vz = video @ C_z + b_z
        vr = video @ C_r + b_r
        vh = video @ C + b
        xz = jnp.einsum('btd,de->bte', seq, W_z)
        xr = jnp.einsum('btd,de->bte', seq, W_r)
        xh = jnp.einsum('btd,de->bte', seq, W)

        def step(h, xs):
            xzt, xrt, xht = xs
            z = jax.nn.sigmoid(xzt + h @ U_z + vz)
            r = jax.nn.sigmoid(xrt + h @ U_r + vr)
            hh = jnp.tanh(xht + r * h @ U + vh)
            h_new = (1.0 - z) * h + z * hh
            return (h_new, h_new)
        h0 = jnp.zeros((seq.shape[0], U.shape[0]), seq.dtype)
        xs = (jnp.swapaxes(xz, 0, 1), jnp.swapaxes(xr, 0, 1), jnp.swapaxes(xh, 0, 1))
        _, out_t = jax.lax.scan(step, h0, xs)
        return jnp.swapaxes(out_t, 0, 1)
    x = x + _L0_cond_ref(x, cond_1024, L0_cond_W1, L0_cond_b1, L0_cond_W2, L0_cond_b2)
    x = x + _L1_cond_ref(cond_1024, x, L1_cond_W_z, L1_cond_U_z, L1_cond_C_z, L1_cond_b_z, L1_cond_W_r, L1_cond_U_r, L1_cond_C_r, L1_cond_b_r, L1_cond_W, L1_cond_U, L1_cond_C, L1_cond_b)
    return x

_drawn_inputs = setup_inputs


def setup_inputs(seed=0):
    import zlib

    import numpy as np

    out = dict(_drawn_inputs(seed))
    spreads = {'L0_cond_b1': (0.0, 0.8),
     'L0_cond_b2': (0.0, 0.8),
     'L1_cond_b_z': (0.0, 0.8),
     'L1_cond_b_r': (0.0, 2.0),
     'L1_cond_b': (0.0, 0.285)}
    factors = {'L1_cond_U_z': 8.0,
     'L1_cond_C_z': 5.675,
     'L1_cond_W_r': 8.0,
     'L1_cond_U_r': 44.177,
     'L1_cond_C_r': 8.0,
     'L1_cond_U': 5.69}
    for name, (base, spread) in spreads.items():
        noise = np.random.default_rng([zlib.crc32(name.encode()), seed]).standard_normal(out[name].shape)
        drawn = base * np.exp(spread * noise) if base else spread * noise
        out[name] = jnp.asarray(drawn.astype(out[name].dtype))
    for name, factor in factors.items():
        out[name] = (out[name] * factor).astype(out[name].dtype)
    return out
```

```python
from contextlib import ExitStack

import concourse.bass as bass
from concourse import mybir

ALU = mybir.AluOpType
ACT = mybir.ActivationFunctionType
F32 = mybir.dt.float32
F16 = mybir.dt.float16
I32 = mybir.dt.int32
AX_X = mybir.AxisListType.X
RMAX = bass.bass_isa.ReduceOp.max

P = 128
R, Z, H = 0, 1, 2
H_SCALE = 2.0 ** 13
EXP_MASK = 0x7F800000


def gru_kernel(nc, x, cond, W1, b1, W2, b2, W_z, U_z, C_z, b_z, W_r, U_r, C_r, b_r, W, U, C, b, out):
    B, T, D = x.shape
    K = D // P
    S = K * B
    HC = K // 2
    HS = S // 2
    TB = P // B
    NB = T // TB
    UN = 4
    G = 3

    with ExitStack() as ctx:
        def sb(name, shape, dt=F32):
            return ctx.enter_context(nc.sbuf_tensor(name, shape, dt))

        def psum(name):
            return ctx.enter_context(nc.psum_tensor(name, [P, 512], F32))

        def sem(name):
            return ctx.enter_context(nc.semaphore(name))

        ident = sb("ident", [P, P])
        w_in = sb("w_in", [P, G, K, D])
        u_raw = sb("u_raw", [P, G, K, D])
        u_part = sb("u_part", [P, G, 2, K, D], F16)
        c_in = sb("c_in", [P, G, K, D])
        mlp_w = sb("mlp_w", [P, 2, K, D])
        mlp_wT = sb("mlp_wT", [P, 2, K, D])
        condT = sb("condT", [P, K, B])
        bias_in = sb("bias_in", [P, 5, K])
        mlp_pre = sb("mlp_pre", [P, 2, S])
        mlp_tanh = sb("mlp_tanh", [P, 2, S])
        mlp_sig = sb("mlp_sig", [P, 2, S])
        hidden = sb("hidden", [P, S])
        gate2 = sb("gate2", [P, S])
        v_bias = sb("v_bias", [P, G, S])
        u_max = sb("u_max", [P, G])
        u_all = sb("u_all", [P, G])
        u_lim = sb("u_lim", [P, G])
        u_pow = sb("u_pow", [P, G])
        u_inv = sb("u_inv", [P, G])
        u_scale = sb("u_scale", [P, G])
        unscale = sb("unscale", [P, G])
        x_tok = sb("x_tok", [P, D])
        yT = sb("yT", [P, S, TB])
        xp = sb("xp", [P, G, TB, S])
        hist = sb("hist", [P, TB, S])
        oT = sb("oT", [P, S, TB])
        o_tok = sb("o_tok", [P, D])
        h_cur = sb("h_cur", [P, S])
        h_part = sb("h_part", [P, K, 2, B], F16)
        rh = sb("rh", [P, S])
        rh_part = sb("rh_part", [P, K, 2, B], F16)
        pre1 = sb("pre1", [P, G, S])
        pre2 = sb("pre2", [P, G, S])
        th = sb("th", [P, G, S])
        one_minus_z = sb("one_minus_z", [P, S])
        keep = sb("keep", [P, S])
        take = sb("take", [P, S])
        zn = sb("zn", [P, S])

        ps_r, ps_z, ps_h0, ps_h1, ps_t = (psum(f"ps_{n}") for n in ("r", "z", "h0", "h1", "t"))
        ps_p = [psum(f"ps_p{g}") for g in range(G)]

        names = ("ld_misc ld_mlp ld_u ld_c ld_w cst ident0 "
                 "mlp_tr mlp_ev mlp1_mm mlp1_pre mlp1_th mlp1_sig mlp1_h mlp2_mm mlp2_pre mlp2_th mlp2_sig gate_ok "
                 "v_mm v_ok umax_ok uall_ok usc umul uhi u_ok "
                 "x_in x_tr y_ok proj_mm xp_ok o_sum o_tr o_ev out_st "
                 "r_mm z_mm h0_mm h1_mm r_p1 r_p2 r_th z_p1 z_p2 z_th omz_ok keep_ok take_ok "
                 "rh_hi rh_32 rh_ok h0_p1 h0_p2 h0_th h1_p1 h1_p2 h1_th zn0 zn1 hi0 hi1 hn0 hn1 hs0 hs1 copied")
        s = {n: sem("s_" + n) for n in names.split()}
        block = ctx.enter_context(nc.Block())

        chunked = lambda w: w.rearrange("(c p) n -> p c n", p=P)
        UG = (U_r, U_z, U)
        WG = (W_r, W_z, W)
        CG = (C_r, C_z, C)
        ps_h = (ps_h0, ps_h1)
        half = (slice(0, HS), slice(HS, S))

        @block.sync
        def _(sp):
            for k in range(K):
                sp.dma_start(condT[:, k, :], cond[:, k * P:(k + 1) * P].rearrange("b p -> p b"), allow_slow_non_contiguous=True).then_inc(s["ld_misc"], 16)
            for n, v in enumerate((b1, b2, b_r, b_z, b)):
                sp.dma_start(bias_in[:, n, :], v.rearrange("(c p) -> p c", p=P), allow_slow_non_contiguous=True).then_inc(s["ld_misc"], 16)
            for n, w in enumerate((W1, W2)):
                sp.dma_start(mlp_w[:, n], chunked(w)).then_inc(s["ld_mlp"], 16)
            for n, w in enumerate(UG):
                sp.dma_start(u_raw[:, n], chunked(w)).then_inc(s["ld_u"], 16)
            for n, w in enumerate(CG):
                sp.dma_start(c_in[:, n], chunked(w)).then_inc(s["ld_c"], 16)
            for n, w in enumerate(WG):
                sp.dma_start(w_in[:, n], chunked(w)).then_inc(s["ld_w"], 16)
            for bb in range(B):
                sp.dma_start(x_tok[bb * TB:(bb + 1) * TB, :], x[bb, 0:TB, :]).then_inc(s["x_in"], 16)
            with sp.Fori(0, NB - 1) as n:
                v = sp.snap(n + 1)
                sp.wait_ge(s["x_tr"], v)
                for bb in range(B):
                    sp.dma_start(x_tok[bb * TB:(bb + 1) * TB, :],
                                 x[bb].rearrange("(n t) d -> n t d", t=TB)[v]).then_inc(s["x_in"], 16)
                sp.wait_ge(s["o_ev"], sp.snap(n + 2))
                for bb in range(B):
                    sp.dma_start(out[bb].rearrange("(n t) d -> n t d", t=TB)[n],
                                 o_tok[bb * TB:(bb + 1) * TB, :]).then_inc(s["out_st"], 16)
            sp.wait_ge(s["o_ev"], NB + 1)
            for bb in range(B):
                sp.dma_start(out[bb, T - TB:T, :], o_tok[bb * TB:(bb + 1) * TB, :]).then_inc(s["out_st"], 16)
            sp.wait_ge(s["out_st"], 16 * B * (NB + 1))

        @block.gpsimd
        def _(pool):
            nc.gpsimd.memset(ident[:, :], 0.0).then_inc(s["ident0"], 1)
            pool.wait_ge(s["ident0"], 1)
            nc.gpsimd.affine_select(out=ident[:, :], in_=ident[:, :], compare_op=ALU.not_equal, fill=1.0,
                                    base=0, pattern=[[-1, P]], channel_multiplier=1).then_inc(s["cst"], 1)
            pool.wait_ge(s["umax_ok"], G)
            nc.gpsimd.partition_all_reduce(u_all[:, :], u_max[:, :], P, RMAX).then_inc(s["uall_ok"], 1)

        @block.tensor
        def _(pe):
            pe.wait_ge(s["cst"], 1)
            pe.wait_ge(s["ld_mlp"], 32)
            for n in range(2):
                for ki in range(K):
                    i = n * K + ki
                    if i >= 2:
                        pe.wait_ge(s["mlp_ev"], i - 1)
                    for ko in range(K):
                        last = nc.tensor.transpose(ps_p[i % 2][:, ko * P:(ko + 1) * P],
                                                   mlp_w[:, n, ko, ki * P:(ki + 1) * P], ident[:, :])
                    last.then_inc(s["mlp_tr"], 1)
            pe.wait_ge(s["ld_misc"], 16 * (5 + K))
            pe.wait_ge(s["mlp_ev"], 2 * K)

            def small_product(bank, col, weight, rhs):
                for m in range(K):
                    for k in range(K):
                        last = nc.tensor.matmul(bank[:, col + m * B:col + (m + 1) * B], weight[:, k, m * P:(m + 1) * P],
                                                rhs[:, k, :], start=(k == 0), stop=(k == K - 1))
                return last

            hid3 = hidden[:, :].rearrange("p (k b) -> p k b", b=B)
            small_product(ps_t, 0, mlp_wT[:, 0], condT).then_inc(s["mlp1_mm"], 1)
            pe.wait_ge(s["mlp1_h"], 1)
            small_product(ps_t, 0, mlp_wT[:, 1], hid3).then_inc(s["mlp2_mm"], 1)
            pe.wait_ge(s["ld_c"], 16 * G)
            for g in range(G):
                last = small_product(ps_p[2], g * S, c_in[:, g], condT)
            last.then_inc(s["v_mm"], 1)
            pe.wait_ge(s["v_ok"], 1)
            pe.wait_ge(s["gate_ok"], 1)
            pe.wait_ge(s["ld_w"], 16 * G)
            pe.wait_ge(s["u_ok"], 2 * G)

            def recurrent(bank, g, m, k, parts, start):
                cols = bank.rearrange("p (m c) -> p m c", c=2 * B)[:, m]
                for part in range(2):
                    last = nc.tensor.matmul(cols, u_part[:, g, part, k, MG[g][m]],
                                            parts[:, k, :, :].rearrange("p a b -> p (a b)"),
                                            start=start and part == 0, stop=False, skip_group_check=True)
                return last

            MG = {g: [slice(m * P, (m + 1) * P) for m in range(K)] for g in range(G)}

            with pe.Fori(0, NB) as n:
                nb = pe.snap(n + 1)
                pe.wait_ge(s["x_in"], pe.snap(nb * (16 * B)))
                pe.wait_ge(s["o_ev"], nb)
                for c in range(K):
                    last = nc.tensor.transpose(ps_t[:, c * P:(c + 1) * P], x_tok[:, c * P:(c + 1) * P], ident[:, :])
                last.then_inc(s["x_tr"], 1)
                pe.wait_ge(s["y_ok"], nb)
                for g in range(G):
                    for m in range(K):
                        for k in range(K):
                            last = nc.tensor.matmul(ps_p[g][:, m * P:(m + 1) * P], w_in[:, g, k, m * P:(m + 1) * P],
                                                    yT[:, k * B:(k + 1) * B, :].rearrange("p b t -> p (b t)"),
                                                    start=(k == 0), stop=(k == K - 1))
                    last.then_inc(s["proj_mm"], 1)
                with pe.Fori(0, TB // UN) as j:
                    t0 = pe.snap(n * TB + j * UN)
                    for u in range(UN):
                        t1 = pe.snap(t0 + (u + 1))
                        for k in range(K):
                            if k == 0:
                                pe.wait_ge(s["hs0"], t1)
                            if k == HC:
                                pe.wait_ge(s["hs1"], t1)
                            for m in range(K):
                                last = recurrent(ps_r[:, 0:2 * S], R, m, k, h_part, k == 0 and m == 0)
                        last.then_inc(s["r_mm"], 1)
                        for m in range(K):
                            for k in range(K):
                                last = recurrent(ps_z[:, 0:2 * S], Z, m, k, h_part, k == 0 and m == 0)
                        last.then_inc(s["z_mm"], 1)
                        pe.wait_ge(s["rh_ok"], t1)
                        for hf in range(2):
                            for m in range(HC):
                                for k in range(K):
                                    gm = hf * HC + m
                                    cols = ps_h[hf][:, m * 2 * B:(m + 1) * 2 * B]
                                    for part in range(2):
                                        last = nc.tensor.matmul(
                                            cols, u_part[:, H, part, k, gm * P:(gm + 1) * P],
                                            rh_part[:, k, :, :].rearrange("p a b -> p (a b)"),
                                            start=(m == 0 and k == 0 and part == 0), stop=False, skip_group_check=True)
                            last.then_inc(s[f"h{hf}_mm"], 1)
                pe.wait_ge(s["o_sum"], nb)
                for c in range(K):
                    last = nc.tensor.transpose(ps_t[:, c * P:(c + 1) * P],
                                               oT[:, c * B:(c + 1) * B, :].rearrange("p b t -> p (b t)"), ident[:, :])
                last.then_inc(s["o_tr"], 1)

        @block.scalar
        def _(act):
            act.sem_inc(s["o_ev"], 1)
            act.sem_inc(s["out_st"], 16 * B)
            act.sem_inc(s["copied"], 1)
            for n, nm in enumerate(("mlp1", "mlp2")):
                act.wait_ge(s[nm + "_pre"], 1)
                nc.scalar.activation(mlp_tanh[:, n, :], mlp_pre[:, n, :], ACT.Tanh, scale=0.5).then_inc(s[nm + "_th"], 1)
            act.wait_ge(s["usc"], 1)
            for g in range(G):
                nc.scalar.activation(u_part[:, g, 0], u_raw[:, g], ACT.Copy, scale=u_scale[:, g:g + 1]).then_inc(s["uhi"], 1)

            with act.Fori(0, NB) as n:
                nb = act.snap(n + 1)
                with act.Fori(0, TB // UN) as j:
                    t0 = act.snap(n * TB + j * UN)
                    tl = act.snap(j * UN)
                    for u in range(UN):
                        t1 = act.snap(t0 + (u + 1))
                        act.wait_ge(s["r_p2"], t1)
                        nc.scalar.activation(th[:, R, :], pre2[:, R, :], ACT.Tanh, scale=0.5).then_inc(s["r_th"], 1)
                        act.wait_ge(s["z_p2"], t1)
                        nc.scalar.activation(th[:, Z, :], pre2[:, Z, :], ACT.Tanh, scale=0.5).then_inc(s["z_th"], 1)
                        for hf in range(2):
                            act.wait_ge(s[f"h{hf}_p2"], t1)
                            nc.scalar.activation(th[:, H, half[hf]], pre2[:, H, half[hf]], ACT.Tanh).then_inc(s[f"h{hf}_th"], 1)
                        act.wait_ge(s["hn0"], t1)
                        act.wait_ge(s["hn1"], t1)
                        nc.scalar.activation(hist[:, tl + u, :], h_cur[:, :], ACT.Copy).then_inc(s["copied"], 1)
                act.wait_ge(s["o_tr"], nb)
                act.wait_ge(s["out_st"], act.snap(nb * (16 * B)))
                nc.scalar.activation(o_tok[:, :], ps_t[:, :], ACT.Copy).then_inc(s["o_ev"], 1)

        @block.vector
        def _(dve):
            V = nc.vector
            for i in range(2 * K):
                dve.wait_ge(s["mlp_tr"], i + 1)
                V.tensor_copy(mlp_wT[:, i // K, i % K, :], ps_p[i % 2][:, :]).then_inc(s["mlp_ev"], 1)
            dve.wait_ge(s["ld_misc"], 16 * (5 + K))

            def bcast(v):
                return v.unsqueeze(2).broadcast_to([P, K, B])

            for n, nm in enumerate(("mlp1", "mlp2")):
                dve.wait_ge(s[nm + "_mm"], 1)
                V.tensor_tensor(mlp_pre[:, n, :].rearrange("p (k b) -> p k b", b=B),
                                ps_t[:, 0:S].rearrange("p (k b) -> p k b", b=B), bcast(bias_in[:, n, :]),
                                ALU.add).then_inc(s[nm + "_pre"], 1)
                dve.wait_ge(s[nm + "_th"], 1)
                V.tensor_scalar(mlp_sig[:, n, :], mlp_tanh[:, n, :], 0.5, 0.5, ALU.mult, ALU.add).then_inc(s[nm + "_sig"], 1)
                dve.wait_ge(s[nm + "_sig"], 1)
                if n == 0:
                    dve.wait_ge(s["mlp1_pre"], 1)
                    V.tensor_tensor(hidden[:, :], mlp_pre[:, 0, :], mlp_sig[:, 0, :], ALU.mult).then_inc(s["mlp1_h"], 1)
                else:
                    V.tensor_scalar(gate2[:, :], mlp_sig[:, 1, :], 2.0, None, ALU.add).then_inc(s["gate_ok"], 1)
            dve.wait_ge(s["v_mm"], 1)
            for g in range(G):
                last = V.tensor_tensor(v_bias[:, g, :].rearrange("p (k b) -> p k b", b=B),
                                       ps_p[2][:, g * S:(g + 1) * S].rearrange("p (k b) -> p k b", b=B),
                                       bcast(bias_in[:, 2 + g, :]), ALU.add)
            last.then_inc(s["v_ok"], 1)
            dve.wait_ge(s["ld_u"], 16 * G)
            for g in range(G):
                V.tensor_reduce(u_max[:, g:g + 1], u_raw[:, g].rearrange("p k n -> p (k n)"), AX_X, ALU.max,
                                apply_absolute_value=True).then_inc(s["umax_ok"], 1)
            dve.wait_ge(s["uall_ok"], 1)
            V.tensor_scalar(u_lim[:, :], u_all[:, :], 1e-20, 1e20, ALU.max, ALU.min).then_inc(s["umul"], 1)
            dve.wait_ge(s["umul"], 1)
            V.tensor_scalar(u_pow[:, :].bitcast(I32), u_lim[:, :].bitcast(I32), EXP_MASK, None,
                            ALU.bitwise_and).then_inc(s["umul"], 1)
            dve.wait_ge(s["umul"], 2)
            V.tensor_scalar(u_inv[:, :].bitcast(I32), u_pow[:, :].bitcast(I32), EXP_MASK, None,
                            ALU.bitwise_xor).then_inc(s["umul"], 1)
            for g in range(G):
                V.tensor_scalar(unscale[:, g:g + 1], u_pow[:, g:g + 1], 2.0 ** (-28 if g == H else -27), None, ALU.mult)
            dve.wait_ge(s["umul"], 3)
            V.tensor_scalar(u_scale[:, :], u_inv[:, :], 2.0 ** 13, None, ALU.mult).then_inc(s["usc"], 1)
            dve.wait_ge(s["usc"], 1)
            for g in range(G):
                dve.wait_ge(s["uhi"], g + 1)
                V.scalar_tensor_tensor(u_part[:, g, 1].rearrange("p k n -> p (k n)"),
                                       u_raw[:, g].rearrange("p k n -> p (k n)"), u_scale[:, g:g + 1],
                                       u_part[:, g, 0].rearrange("p k n -> p (k n)"), ALU.mult,
                                       ALU.subtract).then_inc(s["u_ok"], 2)
            V.memset(h_cur[:, :], 0.0)
            V.memset(h_part[:, 0:HC], 0.0).then_inc(s["hs0"], 1)
            V.memset(h_part[:, HC:K], 0.0).then_inc(s["hs1"], 1)

            def pre_sum(bank, g, cols, tl, p1, p2, t1):
                v = bank.rearrange("p (m a b) -> p m a b", a=2, b=B)
                w = lambda a: a.rearrange("p (m b) -> p m b", b=B)
                V.scalar_tensor_tensor(w(pre1[:, g, cols]), v[:, :, 0, :], unscale[:, g:g + 1],
                                       w(xp[:, g, tl, cols]), ALU.mult, ALU.add).then_inc(s[p1], 1)
                dve.wait_ge(s[p1], t1)
                V.scalar_tensor_tensor(w(pre2[:, g, cols]), v[:, :, 1, :], unscale[:, g:g + 1],
                                       w(pre1[:, g, cols]), ALU.mult, ALU.add).then_inc(s[p2], 1)

            kb = lambda a: a.rearrange("p (k b) -> p k b", b=B)
            with dve.Fori(0, NB) as n:
                nb = dve.snap(n + 1)
                dve.wait_ge(s["x_tr"], nb)
                for c in range(S):
                    last = V.tensor_scalar(yT[:, c, :], ps_t[:, c * TB:(c + 1) * TB], gate2[:, c:c + 1], None, ALU.mult)
                last.then_inc(s["y_ok"], 1)
                for g in range(G):
                    dve.wait_ge(s["proj_mm"], dve.snap(n * G + (g + 1)))
                    V.tensor_tensor(xp[:, g].rearrange("p t c -> p c t"), ps_p[g][:, :].rearrange("p (c t) -> p c t", t=TB),
                                    v_bias[:, g, :].unsqueeze(2).broadcast_to([P, S, TB]), ALU.add).then_inc(s["xp_ok"], 1)
                xp_count = dve.snap(nb * G)
                with dve.Fori(0, TB // UN) as j:
                    dve.wait_ge(s["xp_ok"], xp_count)
                    t0 = dve.snap(n * TB + j * UN)
                    tj = dve.snap(j * UN)
                    for u in range(UN):
                        t1 = dve.snap(t0 + (u + 1))
                        tl = tj + u
                        dve.wait_ge(s["r_mm"], t1)
                        pre_sum(ps_r[:, 0:2 * S], R, slice(0, S), tl, "r_p1", "r_p2", t1)
                        dve.wait_ge(s["r_th"], t1)
                        V.scalar_tensor_tensor(rh_part[:, :, 0, :], kb(th[:, R, :]), 1.0, kb(h_cur[:, :]),
                                               ALU.add, ALU.mult).then_inc(s["rh_hi"], 1)
                        V.scalar_tensor_tensor(rh[:, :], th[:, R, :], 1.0, h_cur[:, :],
                                               ALU.add, ALU.mult).then_inc(s["rh_32"], 1)
                        dve.wait_ge(s["rh_hi"], t1)
                        dve.wait_ge(s["rh_32"], t1)
                        V.tensor_tensor(rh_part[:, :, 1, :], kb(rh[:, :]), rh_part[:, :, 0, :],
                                        ALU.subtract).then_inc(s["rh_ok"], 1)
                        dve.wait_ge(s["z_mm"], t1)
                        pre_sum(ps_z[:, 0:2 * S], Z, slice(0, S), tl, "z_p1", "z_p2", t1)
                        dve.wait_ge(s["z_th"], t1)
                        V.tensor_scalar(one_minus_z[:, :], th[:, Z, :], -0.5, 0.5, ALU.mult, ALU.add).then_inc(s["omz_ok"], 1)
                        V.tensor_scalar(take[:, :], th[:, Z, :], 0.5 * H_SCALE, 0.5 * H_SCALE, ALU.mult,
                                        ALU.add).then_inc(s["take_ok"], 1)
                        dve.wait_ge(s["omz_ok"], t1)
                        V.tensor_tensor(keep[:, :], one_minus_z[:, :], h_cur[:, :], ALU.mult).then_inc(s["keep_ok"], 1)
                        for hf in range(2):
                            dve.wait_ge(s[f"h{hf}_mm"], t1)
                            pre_sum(ps_h[hf][:, 0:2 * HS], H, half[hf], tl, f"h{hf}_p1", f"h{hf}_p2", t1)
                        dve.wait_ge(s["take_ok"], t1)
                        dve.wait_ge(s["keep_ok"], t1)
                        dve.wait_ge(s["copied"], t1)
                        for hf in range(2):
                            c, kc = half[hf], slice(hf * HC, (hf + 1) * HC)
                            dve.wait_ge(s[f"h{hf}_th"], t1)
                            V.tensor_tensor(zn[:, c], take[:, c], th[:, H, c], ALU.mult).then_inc(s[f"zn{hf}"], 1)
                            dve.wait_ge(s[f"zn{hf}"], t1)
                            V.tensor_tensor(h_part[:, kc, 0, :], kb(zn[:, c]), kb(keep[:, c]), ALU.add).then_inc(s[f"hi{hf}"], 1)
                            V.tensor_tensor(h_cur[:, c], zn[:, c], keep[:, c], ALU.add).then_inc(s[f"hn{hf}"], 1)
                            dve.wait_ge(s[f"hi{hf}"], t1)
                            dve.wait_ge(s[f"hn{hf}"], t1)
                            V.tensor_tensor(h_part[:, kc, 1, :], kb(h_cur[:, c]), h_part[:, kc, 0, :],
                                            ALU.subtract).then_inc(s[f"hs{hf}"], 1)
                dve.wait_ge(s["copied"], dve.snap(nb * TB + 1))
                V.scalar_tensor_tensor(oT[:, :, :], hist[:, :, :].rearrange("p t c -> p c t"), 1.0 / H_SCALE, yT[:, :, :],
                                       ALU.mult, ALU.add).then_inc(s["o_sum"], 1)


_INS = ["x", "cond_1024", "L0_cond_W1", "L0_cond_b1", "L0_cond_W2", "L0_cond_b2",
        "L1_cond_W_z", "L1_cond_U_z", "L1_cond_C_z", "L1_cond_b_z",
        "L1_cond_W_r", "L1_cond_U_r", "L1_cond_C_r", "L1_cond_b_r",
        "L1_cond_W", "L1_cond_U", "L1_cond_C", "L1_cond_b"]


def kernel(**inputs):
    import numpy as _np
    import concourse.bacc as _bacc
    from concourse import mybir as _mybir
    from concourse.bass_utils import run_bass_kernel_spmd as _run

    nc = _bacc.Bacc("TRN2", target_bir_lowering=False, num_devices=1)
    arrays, args = {}, []
    for name in _INS:
        a = _np.ascontiguousarray(inputs[name])
        arrays[f"in_{name}"] = a
        args.append(nc.dram_tensor(f"in_{name}", a.shape, _mybir.dt.from_np(a.dtype), kind="ExternalInput").ap())
    shape = inputs["x"].shape
    args.append(nc.dram_tensor("out_dram", shape, _mybir.dt.float32, kind="ExternalOutput").ap())
    gru_kernel(nc, *args)
    r = _run(nc, [arrays], core_ids=[0])
    return r.results[0]["out_dram"]
```

```python
from contextlib import ExitStack

import concourse.bass as bass
from concourse import mybir

ALU = mybir.AluOpType
ACT = mybir.ActivationFunctionType
F32 = mybir.dt.float32
F16 = mybir.dt.float16
I32 = mybir.dt.int32
AX_X = mybir.AxisListType.X
RMAX = bass.bass_isa.ReduceOp.max

P = 128
R, Z, H = 0, 1, 2
H_SCALE = 2.0 ** 13
EXP_MASK = 0x7F800000


def gru_kernel(nc, x, cond, W1, b1, W2, b2, W_z, U_z, C_z, b_z, W_r, U_r, C_r, b_r, W, U, C, b, out):
    B, T, D = x.shape
    K = D // P
    S = K * B
    HC = K // 2
    HS = S // 2
    TB = P // B
    NB = T // TB
    G = 3
    GM = G * K
    UN = 4
    PARTS, ADDENDS = 2, 3
    assert TB // UN >= GM

    with ExitStack() as ctx:
        def sb(name, shape, dt=F32):
            return ctx.enter_context(nc.sbuf_tensor(name, shape, dt))

        def psum(name):
            return ctx.enter_context(nc.psum_tensor(name, [P, 512], F32))

        ident = sb("ident", [P, P])
        w_in = sb("w_in", [P, GM, K, P])
        w_stage = sb("w_stage", [P, K, P])
        u_raw = sb("u_raw", [P, G, K, D])
        u_part = sb("u_part", [P, G, PARTS, K, D], F16)
        c_in = sb("c_in", [P, G, K, D])
        mlp_w = sb("mlp_w", [P, 2, K, D])
        mlp_wT = sb("mlp_wT", [P, 2, K, D])
        condT = sb("condT", [P, K, B])
        bias_in = sb("bias_in", [P, 5, K])
        mlp_pre = sb("mlp_pre", [P, 2, S])
        mlp_tanh = sb("mlp_tanh", [P, 2, S])
        mlp_sig = sb("mlp_sig", [P, 2, S])
        hidden = sb("hidden", [P, S])
        gate2 = sb("gate2", [P, S])
        v_raw = sb("v_raw", [P, G, S])
        v_bias = sb("v_bias", [P, GM, B])
        u_max = sb("u_max", [P, G])
        u_all = sb("u_all", [P, G])
        u_lim = sb("u_lim", [P, G])
        u_pow = sb("u_pow", [P, G])
        u_inv = sb("u_inv", [P, G])
        u_scale = sb("u_scale", [P, G])
        pre_scale = sb("pre_scale", [P, G])
        tanh_scale = sb("tanh_scale", [P, G])
        x_tok = sb("x_tok", [P, D])
        y_next = sb("y_next", [P, S, TB])
        y_cur = sb("y_cur", [P, S, TB])
        xp = sb("xp", [P, GM, 2 * TB, B])
        hist = sb("hist", [P, TB, S])
        oT = sb("oT", [P, S, TB])
        o_tok = sb("o_tok", [P, D])
        h_cur = sb("h_cur", [P, S])
        h_part = sb("h_part", [P, K, PARTS, B], F16)
        rh = sb("rh", [P, S])
        rh_part = sb("rh_part", [P, K, PARTS, B], F16)
        one_minus_z = sb("one_minus_z", [P, S])
        keep = sb("keep", [P, S])
        take = sb("take", [P, S])
        zn = sb("zn", [P, S])

        ps_r, ps_z, ps_h0, ps_h1, ps_x, ps_o, ps_p = (psum(f"ps_{n}") for n in ("r", "z", "h0", "h1", "x", "o", "p"))
        SUM, TANH = 64, 96

        def cols(bank, m0, m1):
            return bank[:, ADDENDS * B * m0:ADDENDS * B * m1].rearrange("p (m a b) -> p m a b", a=ADDENDS, b=B)

        names = ("ld_misc ld_mlp ld_u ld_c ld_w ident_zero ident_ok "
                 "mlp_tr mlp_ev mlp1_mm mlp1_pre mlp1_th mlp1_sig mlp1_h mlp2_mm mlp2_pre mlp2_th mlp2_sig gate_ok "
                 "v_mm v_raw_ok v_ok umax_ok uall_ok upow scale_ok uhi u_ok w_ok "
                 "x_in x_tr y_ok y_copied proj0_mm proj0_ok wst_in proj_mm proj_ok o_sum o_tr o_ev out_st "
                 "seed0 h0_ready r_mm z_mm h0_mm h1_mm r_sum z_sum h0_sum h1_sum r_th z_th h0_th h1_th "
                 "omz_ok take_ok rh_32 rh_ok zn0 zn1 hn0 hn1 hs0 hs1 copied")
        s = {n: ctx.enter_context(nc.semaphore("s_" + n)) for n in names.split()}
        block = ctx.enter_context(nc.Block())

        chunked = lambda w: w.rearrange("(c p) n -> p c n", p=P)
        kb = lambda a: a.rearrange("p (k b) -> p k b", b=B)
        UG, WG, CG = (U_r, U_z, U), (W_r, W_z, W), (C_r, C_z, C)
        ps_h = (ps_h0, ps_h1)
        half = (slice(0, HS), slice(HS, S))
        BYTES = 16 * B

        @block.sync
        def _(sp):
            for k in range(K):
                sp.dma_start(condT[:, k, :], cond[:, k * P:(k + 1) * P].rearrange("b p -> p b"),
                             allow_slow_non_contiguous=True).then_inc(s["ld_misc"], 16)
            for n, v in enumerate((b1, b2, b_r, b_z, b)):
                sp.dma_start(bias_in[:, n, :], v.rearrange("(c p) -> p c", p=P),
                             allow_slow_non_contiguous=True).then_inc(s["ld_misc"], 16)
            for n, w in enumerate(UG):
                sp.dma_start(u_raw[:, n], chunked(w)).then_inc(s["ld_u"], 16)
            for n, w in enumerate((W1, W2)):
                sp.dma_start(mlp_w[:, n], chunked(w)).then_inc(s["ld_mlp"], 16)
            for n, w in enumerate(WG):
                for m in range(K):
                    sp.dma_start(w_in[:, n * K + m], chunked(w)[:, :, m * P:(m + 1) * P]).then_inc(s["ld_w"], 16)
            for n, w in enumerate(CG):
                sp.dma_start(c_in[:, n], chunked(w)).then_inc(s["ld_c"], 16)
            xb = [x[bb].rearrange("(n t) d -> n t d", t=TB) for bb in range(B)]
            ob = [out[bb].rearrange("(n t) d -> n t d", t=TB) for bb in range(B)]

            def load_x(n):
                for bb in range(B):
                    sp.dma_start(x_tok[bb * TB:(bb + 1) * TB, :], xb[bb][n]).then_inc(s["x_in"], 16)

            def store_out(n):
                for bb in range(B):
                    sp.dma_start(ob[bb][n], o_tok[bb * TB:(bb + 1) * TB, :]).then_inc(s["out_st"], 16)

            load_x(0)
            sp.wait_ge(s["x_tr"], 1)
            load_x(1)
            sp.wait_ge(s["w_ok"], G)
            with sp.Fori(0, NB - 1) as n:
                nb = sp.snap(n + 1)
                with sp.Fori(0, GM) as i:
                    sp.wait_ge(s["proj_mm"], sp.snap(n * GM + i + 1))
                    sp.dma_start(w_stage[:, :, :], w_in[:, i]).then_inc(s["wst_in"], 16)
                sp.wait_ge(s["x_tr"], sp.snap(n + 2))
                load_x(sp.snap((n + 2) % NB))
                sp.wait_ge(s["o_ev"], nb)
                store_out(n)
            sp.wait_ge(s["o_ev"], NB)
            store_out(NB - 1)
            sp.wait_ge(s["x_in"], BYTES * (NB + 1))
            sp.wait_ge(s["out_st"], BYTES * (NB + 1))

        @block.gpsimd
        def _(pool):
            nc.gpsimd.memset(ident[:, :], 0.0).then_inc(s["ident_zero"], 1)
            pool.wait_ge(s["ident_zero"], 1)
            nc.gpsimd.affine_select(out=ident[:, :], in_=ident[:, :], compare_op=ALU.not_equal, fill=1.0,
                                    base=0, pattern=[[-1, P]], channel_multiplier=1).then_inc(s["ident_ok"], 1)
            pool.wait_ge(s["umax_ok"], G)
            nc.gpsimd.partition_all_reduce(u_all[:, :], u_max[:, :], P, RMAX).then_inc(s["uall_ok"], 1)

        @block.tensor
        def _(pe):
            pe.wait_ge(s["ident_ok"], 1)

            def transpose_block(bank, src):
                for c in range(K):
                    last = nc.tensor.transpose(bank[:, c * P:(c + 1) * P], src(c), ident[:, :])
                return last

            pe.wait_ge(s["ld_mlp"], 32)
            for n in range(2):
                for ki in range(K):
                    i = n * K + ki
                    if i >= 2:
                        pe.wait_ge(s["mlp_ev"], i - 1)
                    transpose_block((ps_x, ps_p)[i % 2],
                                    lambda c: mlp_w[:, n, c, ki * P:(ki + 1) * P]).then_inc(s["mlp_tr"], 1)
            pe.wait_ge(s["ld_misc"], 16 * (5 + K))
            pe.wait_ge(s["mlp_ev"], 2 * K)

            def small_product(bank, col, weight, rhs):
                for m in range(K):
                    for k in range(K):
                        last = nc.tensor.matmul(bank[:, col + m * B:col + (m + 1) * B], weight[:, k, m * P:(m + 1) * P],
                                                rhs[:, k, :], start=(k == 0), stop=(k == K - 1))
                return last

            small_product(ps_o, 0, mlp_wT[:, 0], condT).then_inc(s["mlp1_mm"], 1)
            pe.wait_ge(s["mlp1_h"], 1)
            small_product(ps_o, 0, mlp_wT[:, 1], kb(hidden[:, :])).then_inc(s["mlp2_mm"], 1)
            pe.wait_ge(s["x_in"], BYTES)
            transpose_block(ps_x, lambda c: x_tok[:, c * P:(c + 1) * P]).then_inc(s["x_tr"], 1)
            pe.wait_ge(s["ld_c"], 16 * G)
            for g in range(G):
                last = small_product(ps_p, g * S, c_in[:, g], condT)
            last.then_inc(s["v_mm"], 1)

            def projection(bank, col, weight, k):
                return nc.tensor.matmul(bank[:, col:col + P], weight[:, k, :],
                                        y_next[:, k * B:(k + 1) * B, :].rearrange("p b t -> p (b t)"),
                                        start=(k == 0), stop=(k == K - 1))

            pe.wait_ge(s["w_ok"], G)
            pe.wait_ge(s["y_ok"], 1)
            pe.wait_ge(s["v_raw_ok"], 1)
            pe.wait_ge(s["gate_ok"], 1)
            for g, bank in enumerate((ps_x, ps_o, ps_p)):
                for m in range(K):
                    for k in range(K):
                        last = projection(bank, m * P, w_in[:, g * K + m], k)
                last.then_inc(s["proj0_mm"], 1)
            pe.wait_ge(s["u_ok"], G)
            pe.wait_ge(s["seed0"], 4)
            pe.wait_ge(s["h0_ready"], 1)

            def tile_product(bank, m, g, gm, k, parts, first):
                for part in range(PARTS):
                    last = nc.tensor.matmul(cols(bank, m, m + 1)[:, 0, 0:PARTS, :].rearrange("p a b -> p (a b)"),
                                            u_part[:, g, part, k, gm * P:(gm + 1) * P],
                                            parts[:, k, :, :].rearrange("p a b -> p (a b)"),
                                            start=first and part == 0, stop=False, skip_group_check=True)
                return last

            def steps(t0, proj):
                for u in range(UN):
                    t1 = pe.snap(t0 + (u + 1))
                    for k in range(K):
                        if k % HC == 0:
                            pe.wait_ge(s[f"hs{k // HC}"], t1)
                        for m in range(K):
                            last = tile_product(ps_r, m, R, m, k, h_part, k == 0 and m == 0)
                    last.then_inc(s["r_mm"], 1)
                    for m in range(K):
                        for k in range(K):
                            last = tile_product(ps_z, m, Z, m, k, h_part, k == 0 and m == 0)
                    last.then_inc(s["z_mm"], 1)
                    pe.wait_ge(s["rh_ok"], t1)
                    for hf in range(2):
                        for m in range(HC):
                            for k in range(K):
                                last = tile_product(ps_h[hf], m, H, hf * HC + m, k, rh_part, k == 0 and m == 0)
                        last.then_inc(s[f"h{hf}_mm"], 1)
                    for k in {0: (0,), 1: (1,), 2: (2, 3)}.get(u, ()) if proj is not None else ():
                        if k == 0:
                            pe.wait_ge(s["wst_in"], proj[0])
                            pe.wait_ge(s["y_ok"], proj[1])
                        last = projection(ps_p, 0, w_stage, k)
                        if k == K - 1:
                            last.then_inc(s["proj_mm"], 1)

            def put_out(nb):
                pe.wait_ge(s["o_sum"], nb)
                transpose_block(ps_o, lambda c: oT[:, c * B:(c + 1) * B, :].rearrange("p b t -> p (b t)"))\
                    .then_inc(s["o_tr"], 1)

            with pe.Fori(0, NB - 1) as n:
                pe.wait_ge(s["x_in"], pe.snap(n * BYTES + 2 * BYTES))
                transpose_block(ps_x, lambda c: x_tok[:, c * P:(c + 1) * P]).then_inc(s["x_tr"], 1)
                y_count = pe.snap(n + 2)
                with pe.Fori(0, GM) as i:
                    steps(pe.snap(n * TB + i * UN), (pe.snap((n * GM + i + 1) * 16), y_count))
                with pe.Fori(0, TB // UN - GM) as i:
                    steps(pe.snap(n * TB + i * UN + GM * UN), None)
                put_out(pe.snap(n + 1))
            with pe.Fori(0, TB // UN) as i:
                steps(pe.snap(i * UN + (NB - 1) * TB), None)
            put_out(NB)

        @block.scalar
        def _(act):
            A = nc.scalar.activation
            act.sem_inc(s["out_st"], BYTES)
            for n, nm in enumerate(("mlp1", "mlp2")):
                act.wait_ge(s[nm + "_pre"], 1)
                A(mlp_tanh[:, n, :], mlp_pre[:, n, :], ACT.Tanh, scale=0.5).then_inc(s[nm + "_th"], 1)
            act.wait_ge(s["scale_ok"], 1)
            for g in range(G):
                A(u_part[:, g, 0], u_raw[:, g], ACT.Copy, scale=u_scale[:, g:g + 1]).then_inc(s["uhi"], 1)

            def seed(bank, g, m0, m1, at):
                return A(cols(bank, 0, m1 - m0)[:, :, ADDENDS - 1, :], xp[:, g * K + m0:g * K + m1, at, :], ACT.Copy)

            act.wait_ge(s["proj0_ok"], 2 * G)
            seed(ps_r, R, 0, K, 0).then_inc(s["seed0"], 1)
            seed(ps_z, Z, 0, K, 0).then_inc(s["seed0"], 1)
            seed(ps_h0, H, 0, HC, 0).then_inc(s["seed0"], 1)
            seed(ps_h1, H, HC, K, 0).then_inc(s["seed0"], 1)

            scale_reg = [act.alloc_register(f"tanh_scale_{g}") for g in range(G)]
            for g in range(G):
                act.reg_load(scale_reg[g], tanh_scale[0:1, g:g + 1].bitcast(I32))

            def tanh(bank, g, n, wait, t1, done):
                act.wait_ge(s[wait], t1)
                A(bank[:, TANH:TANH + n], bank[:, SUM:SUM + n], ACT.Tanh, scale=scale_reg[g]).then_inc(s[done], 1)

            def steps(t0, tl):
                for u in range(UN):
                    t1 = act.snap(t0 + (u + 1))
                    nxt = act.snap((t0 + (u + 1)) % (2 * TB))
                    tanh(ps_r, R, S, "r_sum", t1, "r_th")
                    act.wait_ge(s["rh_32"], t1)
                    seed(ps_r, R, 0, K, nxt)
                    tanh(ps_z, Z, S, "z_sum", t1, "z_th")
                    act.wait_ge(s["take_ok"], t1)
                    seed(ps_z, Z, 0, K, nxt)
                    tanh(ps_h0, H, HS, "h0_sum", t1, "h0_th")
                    tanh(ps_h1, H, HS, "h1_sum", t1, "h1_th")
                    act.wait_ge(s["zn1"], t1)
                    seed(ps_h0, H, 0, HC, nxt)
                    seed(ps_h1, H, HC, K, nxt)
                    act.wait_ge(s["hn1"], t1)
                    A(hist[:, tl + u, :], h_cur[:, :], ACT.Copy).then_inc(s["copied"], 1)

            def begin(nb):
                act.wait_ge(s["y_ok"], nb)
                A(y_cur[:, :, :], y_next[:, :, :], ACT.Copy).then_inc(s["y_copied"], 1)

            def put_out(nb):
                act.wait_ge(s["o_tr"], nb)
                act.wait_ge(s["out_st"], nb * BYTES if isinstance(nb, int) else act.snap(nb * BYTES))
                A(o_tok[:, :], ps_o[:, :], ACT.Copy).then_inc(s["o_ev"], 1)

            with act.Fori(0, NB - 1) as n:
                begin(act.snap(n + 1))
                with act.Fori(0, TB // UN) as i:
                    steps(act.snap(n * TB + i * UN), act.snap(i * UN))
                put_out(act.snap(n + 1))
            begin(NB)
            with act.Fori(0, TB // UN) as i:
                steps(act.snap(i * UN + (NB - 1) * TB), act.snap(i * UN))
            put_out(NB)

        @block.vector
        def _(dve):
            V = nc.vector
            dve.wait_ge(s["ld_u"], 16 * G)
            for g in range(G):
                V.tensor_reduce(u_max[:, g:g + 1], u_raw[:, g].rearrange("p k n -> p (k n)"), AX_X, ALU.max,
                                apply_absolute_value=True).then_inc(s["umax_ok"], 1)
            dve.wait_ge(s["uall_ok"], 1)
            V.tensor_scalar(u_lim[:, :], u_all[:, :], 1e-20, 1e20, ALU.max, ALU.min).then_inc(s["upow"], 1)
            dve.wait_ge(s["upow"], 1)
            V.tensor_scalar(u_pow[:, :].bitcast(I32), u_lim[:, :].bitcast(I32), EXP_MASK, None,
                            ALU.bitwise_and).then_inc(s["upow"], 1)
            dve.wait_ge(s["upow"], 2)
            V.tensor_scalar(u_inv[:, :].bitcast(I32), u_pow[:, :].bitcast(I32), EXP_MASK, None,
                            ALU.bitwise_xor).then_inc(s["upow"], 1)
            for g in range(G):
                V.tensor_scalar(tanh_scale[:, g:g + 1], u_pow[:, g:g + 1], 2.0 ** -28, None, ALU.mult)
            dve.wait_ge(s["upow"], 3)
            for g in range(G):
                V.tensor_scalar(pre_scale[:, g:g + 1], u_inv[:, g:g + 1], 2.0 ** (27 if g == H else 26), None, ALU.mult)
            V.tensor_scalar(u_scale[:, :], u_inv[:, :], 2.0 ** 13, None, ALU.mult).then_inc(s["scale_ok"], 1)
            dve.wait_ge(s["ld_w"], 16 * GM)
            dve.wait_ge(s["scale_ok"], 1)
            for g in range(G):
                wg = w_in[:, g * K:(g + 1) * K].rearrange("p m k n -> p (m k n)")
                V.tensor_scalar(wg, wg, pre_scale[:, g:g + 1], None, ALU.mult).then_inc(s["w_ok"], 1)
            for i in range(2 * K):
                dve.wait_ge(s["mlp_tr"], i + 1)
                V.tensor_copy(mlp_wT[:, i // K, i % K, :], (ps_x, ps_p)[i % 2][:, :]).then_inc(s["mlp_ev"], 1)
            dve.wait_ge(s["ld_misc"], 16 * (5 + K))

            def bcast(v):
                return v.unsqueeze(2).broadcast_to([P, K, B])

            for n, nm in enumerate(("mlp1", "mlp2")):
                dve.wait_ge(s[nm + "_mm"], 1)
                V.tensor_tensor(kb(mlp_pre[:, n, :]), kb(ps_o[:, 0:S]), bcast(bias_in[:, n, :]),
                                ALU.add).then_inc(s[nm + "_pre"], 1)
                dve.wait_ge(s[nm + "_th"], 1)
                V.tensor_scalar(mlp_sig[:, n, :], mlp_tanh[:, n, :], 0.5, 0.5, ALU.mult, ALU.add).then_inc(s[nm + "_sig"], 1)
                dve.wait_ge(s[nm + "_sig"], 1)
                if n == 0:
                    dve.wait_ge(s["mlp1_pre"], 1)
                    V.tensor_tensor(hidden[:, :], mlp_pre[:, 0, :], mlp_sig[:, 0, :], ALU.mult).then_inc(s["mlp1_h"], 1)
                else:
                    V.tensor_scalar(gate2[:, :], mlp_sig[:, 1, :], 2.0, None, ALU.add).then_inc(s["gate_ok"], 1)
            dve.wait_ge(s["gate_ok"], 1)

            def make_y(nb):
                dve.wait_ge(s["x_tr"], nb)
                for c in range(S):
                    last = V.tensor_scalar(y_next[:, c, :], ps_x[:, c * TB:(c + 1) * TB], gate2[:, c:c + 1], None, ALU.mult)
                last.then_inc(s["y_ok"], 1)

            make_y(1)
            dve.wait_ge(s["v_mm"], 1)
            for g in range(G):
                last = V.tensor_tensor(kb(v_raw[:, g, :]), kb(ps_p[:, g * S:(g + 1) * S]), bcast(bias_in[:, 2 + g, :]), ALU.add)
            last.then_inc(s["v_raw_ok"], 1)
            dve.wait_ge(s["v_raw_ok"], 1)
            for g in range(G):
                last = V.tensor_scalar(v_bias[:, g * K:(g + 1) * K, :], kb(v_raw[:, g, :]), pre_scale[:, g:g + 1], None, ALU.mult)
            last.then_inc(s["v_ok"], 1)
            for g in range(G):
                dve.wait_ge(s["uhi"], g + 1)
                flat = lambda a: a.rearrange("p k n -> p (k n)")
                V.scalar_tensor_tensor(flat(u_part[:, g, 1]), flat(u_raw[:, g]), u_scale[:, g:g + 1],
                                       flat(u_part[:, g, 0]), ALU.mult, ALU.subtract).then_inc(s["u_ok"], 1)
            dve.wait_ge(s["v_ok"], 1)
            for g, bank in enumerate((ps_x, ps_o, ps_p)):
                dve.wait_ge(s["proj0_mm"], g + 1)
                src = bank[:, :].rearrange("p (m b t) -> p m t b", b=B, t=TB)
                for bb in range(B):
                    V.tensor_tensor(xp[:, g * K:(g + 1) * K, 0:TB, bb], src[:, :, :, bb],
                                    v_bias[:, g * K:(g + 1) * K, bb:bb + 1].broadcast_to([P, K, TB]),
                                    ALU.add).then_inc(s["proj0_ok"], 1)
            V.memset(h_cur[:, :], 0.0)
            V.memset(h_part[:, 0:HC], 0.0).then_inc(s["hs0"], 1)
            V.memset(h_part[:, HC:K], 0.0).then_inc(s["hs1"], 1)
            V.memset(xp[:, :, TB:2 * TB, :], 0.0).then_inc(s["h0_ready"], 1)
            dve.wait_ge(s["h0_ready"], 1)
            dve.sem_inc(s["proj_mm"], 1)

            def total(bank, m, done):
                return V.tensor_reduce(bank[:, SUM:SUM + m * B].rearrange("p (m b) -> p m b", b=B),
                                       cols(bank, 0, m).rearrange("p m a b -> p m b a"), AX_X, ALU.add).then_inc(s[done], 1)

            def step(t1):
                dve.wait_ge(s["r_mm"], t1)
                total(ps_r, K, "r_sum")
                dve.wait_ge(s["r_th"], t1)
                V.scalar_tensor_tensor(rh_part[:, :, 0, :], kb(ps_r[:, TANH:TANH + S]), 1.0, kb(h_cur[:, :]), ALU.add, ALU.mult)
                V.scalar_tensor_tensor(rh[:, :], ps_r[:, TANH:TANH + S], 1.0, h_cur[:, :],
                                       ALU.add, ALU.mult).then_inc(s["rh_32"], 1)
                dve.wait_ge(s["rh_32"], t1)
                V.tensor_tensor(rh_part[:, :, 1, :], kb(rh[:, :]), rh_part[:, :, 0, :], ALU.subtract).then_inc(s["rh_ok"], 1)
                dve.wait_ge(s["z_mm"], t1)
                total(ps_z, K, "z_sum")
                dve.wait_ge(s["z_th"], t1)
                V.tensor_scalar(one_minus_z[:, :], ps_z[:, TANH:TANH + S], -0.5, 0.5, ALU.mult, ALU.add).then_inc(s["omz_ok"], 1)
                V.tensor_scalar(take[:, :], ps_z[:, TANH:TANH + S], 0.5 * H_SCALE, 0.5 * H_SCALE, ALU.mult,
                                ALU.add).then_inc(s["take_ok"], 1)
                dve.wait_ge(s["omz_ok"], t1)
                V.tensor_tensor(keep[:, :], one_minus_z[:, :], h_cur[:, :], ALU.mult)
                dve.wait_ge(s["h0_mm"], t1)
                total(ps_h0, HC, "h0_sum")

                def take_new(hf):
                    dve.wait_ge(s[f"h{hf}_th"], t1)
                    V.tensor_tensor(zn[:, half[hf]], take[:, half[hf]], ps_h[hf][:, TANH:TANH + HS],
                                    ALU.mult).then_inc(s[f"zn{hf}"], 1)

                def new_state(hf):
                    dve.wait_ge(s[f"zn{hf}"], t1)
                    c, kc = half[hf], slice(hf * HC, (hf + 1) * HC)
                    V.tensor_tensor(h_part[:, kc, 0, :], kb(zn[:, c]), kb(keep[:, c]), ALU.add)
                    V.tensor_tensor(h_cur[:, c], zn[:, c], keep[:, c], ALU.add).then_inc(s[f"hn{hf}"], 1)

                def low_part(hf):
                    dve.wait_ge(s[f"hn{hf}"], t1)
                    c, kc = half[hf], slice(hf * HC, (hf + 1) * HC)
                    V.tensor_tensor(h_part[:, kc, 1, :], kb(h_cur[:, c]), h_part[:, kc, 0, :],
                                    ALU.subtract).then_inc(s[f"hs{hf}"], 1)

                dve.wait_ge(s["h1_mm"], t1)
                total(ps_h1, HC, "h1_sum")
                take_new(0)
                new_state(0)
                take_new(1)
                low_part(0)
                new_state(1)
                low_part(1)

            def store_projection(count, i, ring):
                dve.wait_ge(s["proj_mm"], count)
                V.tensor_tensor(xp[:, i, bass.ds(ring, TB), :].rearrange("p t b -> p b t"),
                                ps_p[:, 0:P].rearrange("p (b t) -> p b t", t=TB),
                                v_bias[:, i, :].unsqueeze(2).broadcast_to([P, B, TB]), ALU.add).then_inc(s["proj_ok"], 1)

            def steps(t0, proj=None):
                for u in range(UN):
                    step(dve.snap(t0 + (u + 1)))
                    if proj is not None and u == 2:
                        store_projection(*proj)

            def put_out(nb, copied):
                dve.wait_ge(s["copied"], copied)
                V.scalar_tensor_tensor(oT[:, :, :], hist[:, :, :].rearrange("p t c -> p c t"), 1.0 / H_SCALE, y_cur[:, :, :],
                                       ALU.mult, ALU.add).then_inc(s["o_sum"], 1)

            with dve.Fori(0, NB - 1) as n:
                dve.wait_ge(s["y_copied"], dve.snap(n + 1))
                make_y(dve.snap(n + 2))
                ring = dve.snap(((n + 1) % 2) * TB)
                with dve.Fori(0, GM) as i:
                    steps(dve.snap(n * TB + i * UN), (dve.snap(n * GM + i + 2), i, ring))
                with dve.Fori(0, TB // UN - GM) as i:
                    steps(dve.snap(n * TB + i * UN + GM * UN))
                put_out(dve.snap(n + 1), dve.snap(n * TB + TB))
            with dve.Fori(0, TB // UN) as i:
                steps(dve.snap(i * UN + (NB - 1) * TB))
            put_out(NB, T)


_INS = ["x", "cond_1024", "L0_cond_W1", "L0_cond_b1", "L0_cond_W2", "L0_cond_b2",
        "L1_cond_W_z", "L1_cond_U_z", "L1_cond_C_z", "L1_cond_b_z",
        "L1_cond_W_r", "L1_cond_U_r", "L1_cond_C_r", "L1_cond_b_r",
        "L1_cond_W", "L1_cond_U", "L1_cond_C", "L1_cond_b"]


def kernel(**inputs):
    import numpy as _np
    import concourse.bacc as _bacc
    from concourse import mybir as _mybir
    from concourse.bass_utils import run_bass_kernel_spmd as _run

    nc = _bacc.Bacc("TRN2", target_bir_lowering=False, num_devices=1)
    arrays, args = {}, []
    for name in _INS:
        a = _np.ascontiguousarray(inputs[name])
        arrays[f"in_{name}"] = a
        args.append(nc.dram_tensor(f"in_{name}", a.shape, _mybir.dt.from_np(a.dtype), kind="ExternalInput").ap())
    shape = inputs["x"].shape
    args.append(nc.dram_tensor("out_dram", shape, _mybir.dt.float32, kind="ExternalOutput").ap())
    gru_kernel(nc, *args)
    r = _run(nc, [arrays], core_ids=[0])
    return r.results[0]["out_dram"]
```

```python
from contextlib import ExitStack

import concourse.bass as bass
from concourse import mybir

ALU = mybir.AluOpType
ACT = mybir.ActivationFunctionType
F32 = mybir.dt.float32
F16 = mybir.dt.float16
I32 = mybir.dt.int32
AX_X = mybir.AxisListType.X
RMAX = bass.bass_isa.ReduceOp.max

P = 128
R, Z, H = 0, 1, 2
H_SCALE = 2.0 ** 13
EXP_MASK = 0x7F800000


def gru_kernel(nc, x, cond, W1, b1, W2, b2, W_z, U_z, C_z, b_z, W_r, U_r, C_r, b_r, W, U, C, b, out):
    B, T, D = x.shape
    K = D // P
    S = K * B
    HC = K // 2
    HS = S // 2
    TB = P // B
    NB = T // TB
    G = 3
    GM = G * K
    PARTS = 2
    ADDENDS = (2 * PARTS + 1, 2 * PARTS + 1, PARTS + 1)
    KEEP, NEW = 0, PARTS
    BODY = TB // GM
    TURN = TB - GM * BODY
    assert BODY > K and TURN >= 3

    with ExitStack() as ctx:
        def sb(name, shape, dt=F32):
            return ctx.enter_context(nc.sbuf_tensor(name, shape, dt))

        def psum(name):
            return ctx.enter_context(nc.psum_tensor(name, [P, 512], F32))

        ident = sb("ident", [P, P])
        w_in = sb("w_in", [P, GM, K, P])
        w_stage = sb("w_stage", [P, K, P])
        u_raw = sb("u_raw", [P, G, K, D])
        u_part = sb("u_part", [P, G, PARTS, K, D], F16)
        c_in = sb("c_in", [P, G, K, D])
        mlp_w = sb("mlp_w", [P, 2, K, D])
        mlp_wT = sb("mlp_wT", [P, 2, K, D])
        condT = sb("condT", [P, K, B])
        bias_in = sb("bias_in", [P, 5, K])
        mlp_pre = sb("mlp_pre", [P, 2, S])
        mlp_tanh = sb("mlp_tanh", [P, 2, S])
        mlp_sig = sb("mlp_sig", [P, 2, S])
        hidden = sb("hidden", [P, S])
        gate2 = sb("gate2", [P, S])
        v_raw = sb("v_raw", [P, G, S])
        v_bias = sb("v_bias", [P, GM, B])
        u_max = sb("u_max", [P, G])
        u_all = sb("u_all", [P, G])
        u_lim = sb("u_lim", [P, G])
        u_pow = sb("u_pow", [P, G])
        u_inv = sb("u_inv", [P, G])
        u_scale = sb("u_scale", [P, G])
        pre_scale = sb("pre_scale", [P, G])
        tanh_scale = sb("tanh_scale", [P, G])
        x_tok = sb("x_tok", [P, D])
        y_next = sb("y_next", [P, S, TB])
        y_cur = sb("y_cur", [P, S, TB])
        xp = sb("xp", [P, GM, 2 * TB, B])
        hist = sb("hist", [P, 2 * TB, S])
        oT = sb("oT", [P, S, TB])
        o_tok = sb("o_tok", [P, D])
        h_cur = sb("h_cur", [P, S])
        h_part = sb("h_part", [P, K, 2 * PARTS, B], F16)
        rh = sb("rh", [P, S])
        rh_part = sb("rh_part", [P, K, PARTS, B], F16)
        th_z = sb("th_z", [P, S])
        z_keep = sb("z_keep", [P, S])
        keep = sb("keep", [P, S])
        z_mul = sb("z_mul", [P, S])
        zn = sb("zn", [P, S])

        ps_z, ps_x, ps_o, ps_p = (psum(f"ps_{n}") for n in ("z", "x", "o", "p"))
        pair_r, pair_h = (ctx.enter_context(nc.psum_tensor(f"pair_{n}", [P, 2, 512], F32)) for n in "rh")
        ps_r, ps_h = ([pair[:, hf, :] for hf in range(2)] for pair in (pair_r, pair_h))
        SUM, TANH = 64, 96

        def cols(bank, g, m0, m1):
            a = ADDENDS[g]
            return bank[:, a * B * m0:a * B * m1].rearrange("p (m a b) -> p m a b", a=a, b=B)

        names = ("ld_misc ld_mlp ld_u ld_c ld_w ident_zero ident_ok "
                 "mlp_tr mlp_ev mlp1_mm mlp1_pre mlp1_th mlp1_sig mlp1_h mlp2_mm mlp2_pre mlp2_th mlp2_sig gate_ok "
                 "v_mm v_raw_ok v_ok umax_ok uall_ok upow scale_ok uhi u_ok w_ok "
                 "x_in x_tr y_ok y_copied proj0_mm proj0_ok wst_in proj_mm o_sum o_tr o_ev out_st "
                 "seed0 h0_ready r0_mm r1_mm z_mm z_keep h_ok h0_mm h1_mm r0_sum r1_sum z_sum h0_sum h1_sum r0_th r1_th z_th h0_th h1_th "
                 "rh32_0 rh32_1 rh0 rh1 keep_ok zn0 zn1 hs0 hs1 copied")
        s = {n: ctx.enter_context(nc.semaphore("s_" + n)) for n in names.split()}
        block = ctx.enter_context(nc.Block())

        chunked = lambda w: w.rearrange("(c p) n -> p c n", p=P)
        kb = lambda a: a.rearrange("p (k b) -> p k b", b=B)
        UG, WG, CG = (U_r, U_z, U), (W_r, W_z, W), (C_r, C_z, C)
        half = (slice(0, HS), slice(HS, S))
        BYTES = 16 * B

        @block.sync
        def _(sp):
            xb = [x[bb].rearrange("(n t) d -> n t d", t=TB) for bb in range(B)]
            ob = [out[bb].rearrange("(n t) d -> n t d", t=TB) for bb in range(B)]

            def load_x(n):
                for bb in range(B):
                    sp.dma_start(x_tok[bb * TB:(bb + 1) * TB, :], xb[bb][n]).then_inc(s["x_in"], 16)

            def store_out(n):
                for bb in range(B):
                    sp.dma_start(ob[bb][n], o_tok[bb * TB:(bb + 1) * TB, :]).then_inc(s["out_st"], 16)

            for n, w in enumerate((W1, W2)):
                sp.dma_start(mlp_w[:, n], chunked(w)).then_inc(s["ld_mlp"], 16)
            for k in range(K):
                sp.dma_start(condT[:, k, :], cond[:, k * P:(k + 1) * P].rearrange("b p -> p b"),
                             allow_slow_non_contiguous=True).then_inc(s["ld_misc"], 16)
            for n, v in enumerate((b1, b2, b_r, b_z, b)):
                sp.dma_start(bias_in[:, n, :], v.rearrange("(c p) -> p c", p=P),
                             allow_slow_non_contiguous=True).then_inc(s["ld_misc"], 16)
            load_x(0)
            for n, w in enumerate(UG):
                sp.dma_start(u_raw[:, n], chunked(w)).then_inc(s["ld_u"], 16)
            for n, w in enumerate(WG):
                for m in range(K):
                    sp.dma_start(w_in[:, n * K + m], chunked(w)[:, :, m * P:(m + 1) * P]).then_inc(s["ld_w"], 16)
            for n, w in enumerate(CG):
                sp.dma_start(c_in[:, n], chunked(w)).then_inc(s["ld_c"], 16)
            sp.wait_ge(s["x_tr"], 1)
            load_x(1)
            sp.wait_ge(s["w_ok"], G)
            with sp.Fori(0, NB) as n:
                sp.wait_ge(s["x_tr"], sp.snap(n + 2))
                load_x(sp.snap((n + 2) % NB))
                sp.wait_ge(s["o_ev"], sp.snap(n + 1))
                store_out(sp.snap((n + (NB - 1)) % NB))
                with sp.Fori(0, GM) as i:
                    sp.wait_ge(s["proj_mm"], sp.snap(n * GM + i + 1))
                    sp.dma_start(w_stage[:, :, :], w_in[:, i]).then_inc(s["wst_in"], 16)
            sp.wait_ge(s["o_ev"], NB + 1)
            store_out(NB - 1)
            sp.wait_ge(s["x_in"], BYTES * (NB + 2))
            sp.wait_ge(s["out_st"], BYTES * (NB + 2))

        @block.gpsimd
        def _(pool):
            nc.gpsimd.memset(ident[:, :], 0.0).then_inc(s["ident_zero"], 1)
            pool.wait_ge(s["ident_zero"], 1)
            nc.gpsimd.affine_select(out=ident[:, :], in_=ident[:, :], compare_op=ALU.not_equal, fill=1.0,
                                    base=0, pattern=[[-1, P]], channel_multiplier=1).then_inc(s["ident_ok"], 1)
            nc.gpsimd.memset(h_cur[:, :], 0.0)
            nc.gpsimd.memset(hist[:, TB:2 * TB, :], 0.0)
            nc.gpsimd.memset(y_cur[:, :, :], 0.0)
            nc.gpsimd.memset(h_part[:, 0:HC], 0.0).then_inc(s["hs0"], 1)
            nc.gpsimd.memset(h_part[:, HC:K], 0.0).then_inc(s["hs1"], 1)
            nc.gpsimd.memset(xp[:, :, TB:2 * TB, :], 0.0).then_inc(s["h0_ready"], 1)
            pool.wait_ge(s["umax_ok"], G)
            nc.gpsimd.partition_all_reduce(u_all[:, :], u_max[:, :], P, RMAX).then_inc(s["uall_ok"], 1)

        @block.tensor
        def _(pe):
            pe.wait_ge(s["ident_ok"], 1)

            def transpose_block(bank, src):
                for c in range(K):
                    last = nc.tensor.transpose(bank[:, c * P:(c + 1) * P], src(c), ident[:, :])
                return last

            pe.wait_ge(s["ld_mlp"], 16 * 2)
            for n in range(2):
                for ki in range(K):
                    i = n * K + ki
                    if i >= 2:
                        pe.wait_ge(s["mlp_ev"], i - 1)
                    transpose_block((ps_x, ps_p)[i % 2],
                                    lambda c: mlp_w[:, n, c, ki * P:(ki + 1) * P]).then_inc(s["mlp_tr"], 1)
            pe.wait_ge(s["ld_misc"], 16 * (5 + K))
            pe.wait_ge(s["mlp_ev"], 2 * K)

            def small_product(bank, col, weight, rhs):
                for m in range(K):
                    for k in range(K):
                        last = nc.tensor.matmul(bank[:, col + m * B:col + (m + 1) * B], weight[:, k, m * P:(m + 1) * P],
                                                rhs[:, k, :], start=(k == 0), stop=(k == K - 1))
                return last

            small_product(ps_o, 0, mlp_wT[:, 0], condT).then_inc(s["mlp1_mm"], 1)
            pe.wait_ge(s["mlp1_h"], 1)
            small_product(ps_o, 0, mlp_wT[:, 1], kb(hidden[:, :])).then_inc(s["mlp2_mm"], 1)
            pe.wait_ge(s["x_in"], BYTES)
            transpose_block(ps_x, lambda c: x_tok[:, c * P:(c + 1) * P]).then_inc(s["x_tr"], 1)

            def projection(bank, col, weight, k):
                return nc.tensor.matmul(bank[:, col:col + P], weight[:, k, :],
                                        y_next[:, k * B:(k + 1) * B, :].rearrange("p b t -> p (b t)"),
                                        start=(k == 0), stop=(k == K - 1))

            pe.wait_ge(s["w_ok"], G)
            pe.wait_ge(s["y_ok"], 1)
            pe.wait_ge(s["gate_ok"], 1)
            for g, bank in enumerate((ps_x, ps_o, ps_p)):
                for m in range(K):
                    for k in range(K):
                        last = projection(bank, m * P, w_in[:, g * K + m], k)
                last.then_inc(s["proj0_mm"], 1)
            pe.wait_ge(s["ld_c"], 16 * G)
            for g in range(G):
                last = small_product(ps_z, g * S, c_in[:, g], condT)
            last.then_inc(s["v_mm"], 1)

            pe.wait_ge(s["u_ok"], G)
            pe.wait_ge(s["seed0"], G)
            pe.wait_ge(s["h0_ready"], 1)

            def tile_product(bank, m, g, gm, k, parts, first):
                for part in range(PARTS):
                    last = nc.tensor.matmul(cols(bank, g, m, m + 1)[:, 0, 0:ADDENDS[g] - 1, :].rearrange("p a b -> p (a b)"),
                                            u_part[:, g, part, k, gm * P:(gm + 1) * P],
                                            parts[:, k, :, :].rearrange("p a b -> p (a b)"),
                                            start=first and part == 0, stop=False, skip_group_check=True)
                return last

            def steps(t0, count, proj=None, turn=None):
                for u in range(count):
                    t1 = pe.snap(t0 + (u + 1))
                    for kh in range(2):
                        pe.wait_ge(s[f"hs{kh}"], t1)
                        for mh in range(2):
                            for m in range(HC):
                                for k in range(kh * HC, (kh + 1) * HC):
                                    last = tile_product(ps_r[mh], m, R, mh * HC + m, k, h_part, k == 0 and m == 0)
                            if kh == 1:
                                last.then_inc(s[f"r{mh}_mm"], 1)
                    for m in range(K):
                        for k in range(K):
                            last = tile_product(ps_z, m, Z, m, k, h_part, k == 0 and m == 0)
                    last.then_inc(s["z_mm"], 1)
                    for mh in range(2):
                        for kh in range(2):
                            if mh == 0:
                                pe.wait_ge(s[f"rh{kh}"], t1)
                            for m in range(HC):
                                for k in range(kh * HC, (kh + 1) * HC):
                                    last = tile_product(ps_h[mh], m, H, mh * HC + m, k, rh_part, k == 0 and m == 0)
                        last.then_inc(s[f"h{mh}_mm"], 1)
                    if proj is not None:
                        if u == 0:
                            pe.wait_ge(s["wst_in"], proj[0])
                            pe.wait_ge(s["y_ok"], proj[1])
                        if u < K:
                            last = projection(ps_p, 0, w_stage, u)
                        if u == K - 1:
                            last.then_inc(s["proj_mm"], 1)
                    if turn is not None and u == 0:
                        pe.wait_ge(s["x_in"], turn[0])
                        transpose_block(ps_x, lambda c: x_tok[:, c * P:(c + 1) * P]).then_inc(s["x_tr"], 1)
                    if turn is not None and u == 1:
                        put_out(turn[1])

            def put_out(nb):
                pe.wait_ge(s["o_sum"], nb)
                transpose_block(ps_o, lambda c: oT[:, c * B:(c + 1) * B, :].rearrange("p b t -> p (b t)"))\
                    .then_inc(s["o_tr"], 1)

            with pe.Fori(0, NB) as n:
                nb = pe.snap(n + 1)
                steps(pe.snap(n * TB), TURN, turn=(pe.snap(n * BYTES + 2 * BYTES), nb))
                y_count = pe.snap(n + 2)
                with pe.Fori(0, GM) as i:
                    steps(pe.snap(n * TB + i * BODY + TURN), BODY, proj=(pe.snap((n * GM + i + 1) * 16), y_count))
            put_out(NB + 1)

        @block.scalar
        def _(act):
            A = nc.scalar.activation
            act.sem_inc(s["out_st"], BYTES)
            for n, nm in enumerate(("mlp1", "mlp2")):
                act.wait_ge(s[nm + "_pre"], 1)
                A(mlp_tanh[:, n, :], mlp_pre[:, n, :], ACT.Tanh, scale=0.5).then_inc(s[nm + "_th"], 1)
            act.wait_ge(s["scale_ok"], 1)
            for g in range(G):
                A(u_part[:, g, 0], u_raw[:, g], ACT.Copy, scale=u_scale[:, g:g + 1]).then_inc(s["uhi"], 1)

            def seed(banks, g, at):
                src = xp[:, g * K:(g + 1) * K, at, :]
                if g == Z:
                    return A(cols(banks, Z, 0, K)[:, :, ADDENDS[Z] - 1, :], src, ACT.Copy)
                a = ADDENDS[g]
                to = banks[:, :, 0:a * HS].rearrange("p h (m a b) -> p h m a b", a=a, b=B)
                return A(to[:, :, :, a - 1, :], src.rearrange("p (h m) b -> p h m b", h=2), ACT.Copy)

            act.wait_ge(s["h0_ready"], 1)
            act.wait_ge(s["proj0_ok"], 2 * G)
            for g, banks in ((R, pair_r), (Z, ps_z), (H, pair_h)):
                seed(banks, g, 0).then_inc(s["seed0"], 1)

            scale_reg = [act.alloc_register(f"tanh_scale_{g}") for g in range(G)]
            for g in range(G):
                act.reg_load(scale_reg[g], tanh_scale[0:1, g:g + 1].bitcast(I32))

            def tanh(to, bank, g, n, wait, t1, done):
                act.wait_ge(s[wait], t1)
                A(to, bank[:, SUM:SUM + n], ACT.Tanh, scale=scale_reg[g]).then_inc(s[done], 1)

            def steps(t0, count, ring, turn=None):
                for u in range(count):
                    t1 = act.snap(t0 + (u + 1))
                    prv = act.snap(ring + (u - 1) if u else (ring + (2 * TB - 1)) % (2 * TB))
                    nxt = act.snap(ring + (u + 1) if u < count - 1 else (ring + count) % (2 * TB))
                    for hf in range(2):
                        tanh(ps_r[hf][:, TANH:TANH + HS], ps_r[hf], R, HS, f"r{hf}_sum", t1, f"r{hf}_th")
                    A(hist[:, prv, :], h_cur[:, :], ACT.Copy)
                    tanh(th_z[:, :], ps_z, Z, S, "z_sum", t1, "z_th")
                    seed(pair_r, R, nxt)
                    act.wait_ge(s["z_th"], t1)
                    A(z_keep[:, :], th_z[:, :], ACT.Copy, scale=-0.5, bias=0.5).then_inc(s["z_keep"], 1)
                    A(z_mul[:, :], th_z[:, :], ACT.Copy, scale=H_SCALE / 2, bias=H_SCALE / 2)
                    tanh(ps_h[0][:, TANH:TANH + HS], ps_h[0], H, HS, "h0_sum", t1, "h0_th")
                    seed(ps_z, Z, nxt)
                    tanh(ps_h[1][:, TANH:TANH + HS], ps_h[1], H, HS, "h1_sum", t1, "h1_th")
                    act.wait_ge(s["zn1"], t1)
                    seed(pair_h, H, nxt)
                    if turn is not None and u == 1:
                        act.wait_ge(s["o_sum"], turn)
                        A(y_cur[:, :, :], y_next[:, :, :], ACT.Copy).then_inc(s["y_copied"], 1)
                    if turn is not None and u == 2:
                        put_out(turn)

            def put_out(nb):
                act.wait_ge(s["o_tr"], nb)
                act.wait_ge(s["out_st"], nb * BYTES if isinstance(nb, int) else act.snap(nb * BYTES))
                A(o_tok[:, :], ps_o[:, :], ACT.Copy).then_inc(s["o_ev"], 1)

            with act.Fori(0, NB) as n:
                steps(act.snap(n * TB), TURN, act.snap((n % 2) * TB), act.snap(n + 1))
                with act.Fori(0, GM) as i:
                    steps(act.snap(n * TB + i * BODY + TURN), BODY, act.snap((n % 2) * TB + i * BODY + TURN))
            act.wait_ge(s["h_ok"], T)
            A(hist[:, (T - 1) % (2 * TB), :], h_cur[:, :], ACT.Copy).then_inc(s["copied"], 1)
            put_out(NB + 1)

        @block.vector
        def _(dve):
            V = nc.vector
            for i in range(2 * K):
                dve.wait_ge(s["mlp_tr"], i + 1)
                V.tensor_copy(mlp_wT[:, i // K, i % K, :], (ps_x, ps_p)[i % 2][:, :]).then_inc(s["mlp_ev"], 1)
            dve.wait_ge(s["ld_misc"], 16 * (5 + K))

            def bcast(v):
                return v.unsqueeze(2).broadcast_to([P, K, B])

            def mlp_layer(n):
                nm = ("mlp1", "mlp2")[n]
                dve.wait_ge(s[nm + "_mm"], 1)
                V.tensor_tensor(kb(mlp_pre[:, n, :]), kb(ps_o[:, 0:S]), bcast(bias_in[:, n, :]),
                                ALU.add).then_inc(s[nm + "_pre"], 1)
                dve.wait_ge(s[nm + "_th"], 1)
                V.tensor_scalar(mlp_sig[:, n, :], mlp_tanh[:, n, :], 0.5, 0.5, ALU.mult, ALU.add).then_inc(s[nm + "_sig"], 1)
                dve.wait_ge(s[nm + "_sig"], 1)
                if n == 0:
                    dve.wait_ge(s["mlp1_pre"], 1)
                    V.tensor_tensor(hidden[:, :], mlp_pre[:, 0, :], mlp_sig[:, 0, :], ALU.mult).then_inc(s["mlp1_h"], 1)
                else:
                    V.tensor_scalar(gate2[:, :], mlp_sig[:, 1, :], 2.0, None, ALU.add).then_inc(s["gate_ok"], 1)

            dve.wait_ge(s["ld_u"], 16 * G)
            for g in range(G):
                V.tensor_reduce(u_max[:, g:g + 1], u_raw[:, g].rearrange("p k n -> p (k n)"), AX_X, ALU.max,
                                apply_absolute_value=True).then_inc(s["umax_ok"], 1)
            mlp_layer(0)
            dve.wait_ge(s["uall_ok"], 1)
            V.tensor_scalar(u_lim[:, :], u_all[:, :], 1e-20, 1e20, ALU.max, ALU.min).then_inc(s["upow"], 1)
            dve.wait_ge(s["upow"], 1)
            V.tensor_scalar(u_pow[:, :].bitcast(I32), u_lim[:, :].bitcast(I32), EXP_MASK, None,
                            ALU.bitwise_and).then_inc(s["upow"], 1)
            dve.wait_ge(s["upow"], 2)
            V.tensor_scalar(u_inv[:, :].bitcast(I32), u_pow[:, :].bitcast(I32), EXP_MASK, None,
                            ALU.bitwise_xor).then_inc(s["upow"], 1)
            for g in range(G):
                V.tensor_scalar(tanh_scale[:, g:g + 1], u_pow[:, g:g + 1], 2.0 ** -28, None, ALU.mult)
            dve.wait_ge(s["upow"], 3)
            for g in range(G):
                V.tensor_scalar(pre_scale[:, g:g + 1], u_inv[:, g:g + 1], 2.0 ** (27 if g == H else 26), None, ALU.mult)
            V.tensor_scalar(u_scale[:, :], u_inv[:, :], 2.0 ** 13, None, ALU.mult).then_inc(s["scale_ok"], 1)
            dve.wait_ge(s["ld_w"], 16 * GM)
            dve.wait_ge(s["scale_ok"], 1)
            for g in range(G):
                wg = w_in[:, g * K:(g + 1) * K].rearrange("p m k n -> p (m k n)")
                V.tensor_scalar(wg, wg, pre_scale[:, g:g + 1], None, ALU.mult).then_inc(s["w_ok"], 1)
            mlp_layer(1)
            dve.wait_ge(s["gate_ok"], 1)

            def make_y(nb):
                dve.wait_ge(s["x_tr"], nb)
                V.tensor_tensor(y_next[:, :, :], ps_x[:, :].rearrange("p (c t) -> p c t", t=TB),
                                gate2[:, :].unsqueeze(2).broadcast_to([P, S, TB]), ALU.mult).then_inc(s["y_ok"], 1)

            make_y(1)
            for g in range(G):
                dve.wait_ge(s["uhi"], g + 1)
                flat = lambda a: a.rearrange("p k n -> p (k n)")
                V.scalar_tensor_tensor(flat(u_part[:, g, 1]), flat(u_raw[:, g]), u_scale[:, g:g + 1],
                                       flat(u_part[:, g, 0]), ALU.mult, ALU.subtract).then_inc(s["u_ok"], 1)
            dve.wait_ge(s["v_mm"], 1)
            for g in range(G):
                last = V.tensor_tensor(kb(v_raw[:, g, :]), kb(ps_z[:, g * S:(g + 1) * S]), bcast(bias_in[:, 2 + g, :]), ALU.add)
            last.then_inc(s["v_raw_ok"], 1)
            dve.wait_ge(s["v_raw_ok"], 1)
            for g in range(G):
                last = V.tensor_scalar(v_bias[:, g * K:(g + 1) * K, :], kb(v_raw[:, g, :]), pre_scale[:, g:g + 1], None, ALU.mult)
            last.then_inc(s["v_ok"], 1)
            dve.wait_ge(s["v_ok"], 1)
            for g, bank in enumerate((ps_x, ps_o, ps_p)):
                dve.wait_ge(s["proj0_mm"], g + 1)
                src = bank[:, :].rearrange("p (m b t) -> p m t b", b=B, t=TB)
                for bb in range(B):
                    V.tensor_tensor(xp[:, g * K:(g + 1) * K, 0:TB, bb], src[:, :, :, bb],
                                    v_bias[:, g * K:(g + 1) * K, bb:bb + 1].broadcast_to([P, K, TB]),
                                    ALU.add).then_inc(s["proj0_ok"], 1)
            dve.wait_ge(s["h0_ready"], 1)
            dve.sem_inc(s["proj_mm"], 1)

            def total(bank, g, m, done):
                return V.tensor_reduce(bank[:, SUM:SUM + m * B].rearrange("p (m b) -> p m b", b=B),
                                       cols(bank, g, 0, m).rearrange("p m a b -> p m b a"), AX_X, ALU.add).then_inc(s[done], 1)

            def step(t1):
                kc = (slice(0, HC), slice(HC, K))

                def gated_high(hf):
                    dve.wait_ge(s[f"r{hf}_th"], t1)
                    V.scalar_tensor_tensor(rh_part[:, kc[hf], 0, :], kb(ps_r[hf][:, TANH:TANH + HS]), 1.0,
                                           kb(h_cur[:, half[hf]]), ALU.add, ALU.mult)

                def gated_full(hf):
                    V.scalar_tensor_tensor(rh[:, half[hf]], ps_r[hf][:, TANH:TANH + HS], 1.0, h_cur[:, half[hf]],
                                           ALU.add, ALU.mult).then_inc(s[f"rh32_{hf}"], 1)

                def gated_low(hf):
                    dve.wait_ge(s[f"rh32_{hf}"], t1)
                    V.tensor_tensor(rh_part[:, kc[hf], 1, :], kb(rh[:, half[hf]]), rh_part[:, kc[hf], 0, :],
                                    ALU.subtract).then_inc(s[f"rh{hf}"], 1)

                for hf in range(2):
                    dve.wait_ge(s[f"r{hf}_mm"], t1)
                    total(ps_r[hf], R, HC, f"r{hf}_sum")
                gated_high(0)
                gated_full(0)
                gated_high(1)
                gated_low(0)
                gated_full(1)
                gated_low(1)
                dve.wait_ge(s["z_mm"], t1)
                total(ps_z, Z, K, "z_sum")
                dve.wait_ge(s["h0_mm"], t1)
                total(ps_h[0], H, HC, "h0_sum")
                dve.wait_ge(s["z_keep"], t1)
                V.tensor_tensor(h_part[:, :, KEEP, :], kb(z_keep[:, :]), kb(h_cur[:, :]), ALU.mult)
                V.tensor_tensor(keep[:, :], z_keep[:, :], h_cur[:, :], ALU.mult).then_inc(s["keep_ok"], 1)

                def keep_low():
                    dve.wait_ge(s["keep_ok"], t1)
                    V.tensor_tensor(h_part[:, :, KEEP + 1, :], kb(keep[:, :]), h_part[:, :, KEEP, :], ALU.subtract)

                def new_high(hf):
                    dve.wait_ge(s[f"h{hf}_th"], t1)
                    V.tensor_tensor(h_part[:, kc[hf], NEW, :], kb(z_mul[:, half[hf]]),
                                    kb(ps_h[hf][:, TANH:TANH + HS]), ALU.mult)

                def new_full(hf):
                    V.tensor_tensor(zn[:, half[hf]], z_mul[:, half[hf]], ps_h[hf][:, TANH:TANH + HS],
                                    ALU.mult).then_inc(s[f"zn{hf}"], 1)

                def new_low(hf):
                    dve.wait_ge(s[f"zn{hf}"], t1)
                    V.tensor_tensor(h_part[:, kc[hf], NEW + 1, :], kb(zn[:, half[hf]]), h_part[:, kc[hf], NEW, :],
                                    ALU.subtract).then_inc(s[f"hs{hf}"], 1)

                new_high(0)
                dve.wait_ge(s["h1_mm"], t1)
                total(ps_h[1], H, HC, "h1_sum")
                new_full(0)
                keep_low()
                new_low(0)
                new_high(1)
                new_full(1)
                new_low(1)
                V.tensor_tensor(h_cur[:, :], keep[:, :], zn[:, :], ALU.add).then_inc(s["h_ok"], 1)

            def store_projection(count, i, ring):
                dve.wait_ge(s["proj_mm"], count)
                V.tensor_tensor(xp[:, i, bass.ds(ring, TB), :].rearrange("p t b -> p b t"),
                                ps_p[:, 0:P].rearrange("p (b t) -> p b t", t=TB),
                                v_bias[:, i, :].unsqueeze(2).broadcast_to([P, B, TB]), ALU.add)

            def make_out(ring):
                V.scalar_tensor_tensor(oT[:, :, :], hist[:, bass.ds(ring, TB), :].rearrange("p t c -> p c t"), 1.0 / H_SCALE,
                                       y_cur[:, :, :], ALU.mult, ALU.add).then_inc(s["o_sum"], 1)

            def steps(t0, count, proj=None, turn=None):
                for u in range(count):
                    step(dve.snap(t0 + (u + 1)))
                    if proj is not None and u == K - 1:
                        store_projection(*proj)
                    if turn is not None and u == 0:
                        make_out(turn[0])
                    if turn is not None and u == 2:
                        dve.wait_ge(s["y_copied"], turn[1])
                        make_y(turn[2])

            with dve.Fori(0, NB) as n:
                other = dve.snap(((n + 1) % 2) * TB)
                steps(dve.snap(n * TB), TURN, turn=(other, dve.snap(n + 1), dve.snap(n + 2)))
                with dve.Fori(0, GM) as i:
                    steps(dve.snap(n * TB + i * BODY + TURN), BODY, proj=(dve.snap(n * GM + i + 2), i, other))
            dve.wait_ge(s["copied"], 1)
            make_out((NB - 1) % 2 * TB)


_INS = ["x", "cond_1024", "L0_cond_W1", "L0_cond_b1", "L0_cond_W2", "L0_cond_b2",
        "L1_cond_W_z", "L1_cond_U_z", "L1_cond_C_z", "L1_cond_b_z",
        "L1_cond_W_r", "L1_cond_U_r", "L1_cond_C_r", "L1_cond_b_r",
        "L1_cond_W", "L1_cond_U", "L1_cond_C", "L1_cond_b"]


def kernel(**inputs):
    import numpy as _np
    import concourse.bacc as _bacc
    from concourse import mybir as _mybir
    from concourse.bass_utils import run_bass_kernel_spmd as _run

    nc = _bacc.Bacc("TRN2", target_bir_lowering=False, num_devices=1)
    arrays, args = {}, []
    for name in _INS:
        a = _np.ascontiguousarray(inputs[name])
        arrays[f"in_{name}"] = a
        args.append(nc.dram_tensor(f"in_{name}", a.shape, _mybir.dt.from_np(a.dtype), kind="ExternalInput").ap())
    shape = inputs["x"].shape
    args.append(nc.dram_tensor("out_dram", shape, _mybir.dt.float32, kind="ExternalOutput").ap())
    gru_kernel(nc, *args)
    r = _run(nc, [arrays], core_ids=[0])
    return r.results[0]["out_dram"]
```
